# Optimizing a Trainium2 kernel written in Bass

```python
import numpy as np
import jax
import jax.numpy as jnp

def _softmax(x, axis=-1):
    return jax.nn.softmax(x, axis=axis)

def _gelu(x):
    return jax.nn.gelu(x, approximate=True)

def _silu(x):
    return jax.nn.silu(x)

def _sigmoid(x):
    return jax.nn.sigmoid(x)

def _layernorm(x, axis=-1, eps=1e-05):
    m = jnp.mean(x, axis=axis, keepdims=True)
    v = jnp.var(x, axis=axis, keepdims=True)
    return (x - m) / jnp.sqrt(v + eps)

def _scatter_add(tgt, idx, src, axis=0):
    return tgt.at[idx].add(src)

def _segment_sum(src, seg, n):
    return jax.ops.segment_sum(src, seg, n)
kernel_name = 'mk_dlrm_tower_d1_rec_r8_af85e1'

def setup_inputs(seed: int=0):
    np.random.seed(seed)
    _w = jnp.asarray

    def _rec_inputs():
        import jax
        import jax.numpy as jnp
        _tk = jax.random.key(seed)
        ids = jnp.stack([jax.random.randint(jax.random.fold_in(_tk, 200 + f), (512,), 0, v, jnp.int32) for f, v in enumerate([12500, 1000, 12500, 1000, 125000, 12500, 1000, 12500, 1250, 1250, 12500, 12500, 12500, 1000, 12500, 12500, 1250, 1250, 1000, 1000, 1000, 1000, 1000, 1000, 1000, 1000])], axis=1)
        tbl_0 = 0.05 * jax.random.normal(jax.random.fold_in(_tk, 500 + 0), (12500, 128), jnp.float32)
        tbl_1 = 0.05 * jax.random.normal(jax.random.fold_in(_tk, 500 + 1), (1000, 128), jnp.float32)
        tbl_2 = 0.05 * jax.random.normal(jax.random.fold_in(_tk, 500 + 2), (12500, 128), jnp.float32)
        tbl_3 = 0.05 * jax.random.normal(jax.random.fold_in(_tk, 500 + 3), (1000, 128), jnp.float32)
        tbl_4 = 0.05 * jax.random.normal(jax.random.fold_in(_tk, 500 + 4), (125000, 128), jnp.float32)
        tbl_5 = 0.05 * jax.random.normal(jax.random.fold_in(_tk, 500 + 5), (12500, 128), jnp.float32)
        tbl_6 = 0.05 * jax.random.normal(jax.random.fold_in(_tk, 500 + 6), (1000, 128), jnp.float32)
        tbl_7 = 0.05 * jax.random.normal(jax.random.fold_in(_tk, 500 + 7), (12500, 128), jnp.float32)
        tbl_8 = 0.05 * jax.random.normal(jax.random.fold_in(_tk, 500 + 8), (1250, 128), jnp.float32)
        tbl_9 = 0.05 * jax.random.normal(jax.random.fold_in(_tk, 500 + 9), (1250, 128), jnp.float32)
        tbl_10 = 0.05 * jax.random.normal(jax.random.fold_in(_tk, 500 + 10), (12500, 128), jnp.float32)
        tbl_11 = 0.05 * jax.random.normal(jax.random.fold_in(_tk, 500 + 11), (12500, 128), jnp.float32)
        tbl_12 = 0.05 * jax.random.normal(jax.random.fold_in(_tk, 500 + 12), (12500, 128), jnp.float32)
        tbl_13 = 0.05 * jax.random.normal(jax.random.fold_in(_tk, 500 + 13), (1000, 128), jnp.float32)
        tbl_14 = 0.05 * jax.random.normal(jax.random.fold_in(_tk, 500 + 14), (12500, 128), jnp.float32)
        tbl_15 = 0.05 * jax.random.normal(jax.random.fold_in(_tk, 500 + 15), (12500, 128), jnp.float32)
        tbl_16 = 0.05 * jax.random.normal(jax.random.fold_in(_tk, 500 + 16), (1250, 128), jnp.float32)
        tbl_17 = 0.05 * jax.random.normal(jax.random.fold_in(_tk, 500 + 17), (1250, 128), jnp.float32)
        tbl_18 = 0.05 * jax.random.normal(jax.random.fold_in(_tk, 500 + 18), (1000, 128), jnp.float32)
        tbl_19 = 0.05 * jax.random.normal(jax.random.fold_in(_tk, 500 + 19), (1000, 128), jnp.float32)
        tbl_20 = 0.05 * jax.random.normal(jax.random.fold_in(_tk, 500 + 20), (1000, 128), jnp.float32)
        tbl_21 = 0.05 * jax.random.normal(jax.random.fold_in(_tk, 500 + 21), (1000, 128), jnp.float32)
        tbl_22 = 0.05 * jax.random.normal(jax.random.fold_in(_tk, 500 + 22), (1000, 128), jnp.float32)
        tbl_23 = 0.05 * jax.random.normal(jax.random.fold_in(_tk, 500 + 23), (1000, 128), jnp.float32)
        tbl_24 = 0.05 * jax.random.normal(jax.random.fold_in(_tk, 500 + 24), (1000, 128), jnp.float32)
        tbl_25 = 0.05 * jax.random.normal(jax.random.fold_in(_tk, 500 + 25), (1000, 128), jnp.float32)
        _rk = jax.random.fold_in(_tk, 7)
        r_dense_features = -0.000520686 + 1.00062 * jax.random.normal(jax.random.fold_in(_rk, 101), (512, 128), jnp.float32)
        W_top1 = 0.0405887 * jax.random.normal(jax.random.fold_in(_tk, 801), (607, 512), jnp.float32)
        W_top2 = 0.0441942 * jax.random.normal(jax.random.fold_in(_tk, 802), (512, 256), jnp.float32)
        W_top3 = 0.0625 * jax.random.normal(jax.random.fold_in(_tk, 803), (256, 1), jnp.float32)
        b_top1 = jnp.zeros((512,), jnp.float32)
        b_top2 = jnp.zeros((256,), jnp.float32)
        return (r_dense_features, ids, tbl_0, tbl_1, tbl_2, tbl_3, tbl_4, tbl_5, tbl_6, tbl_7, tbl_8, tbl_9, tbl_10, tbl_11, tbl_12, tbl_13, tbl_14, tbl_15, tbl_16, tbl_17, tbl_18, tbl_19, tbl_20, tbl_21, tbl_22, tbl_23, tbl_24, tbl_25, W_top1, b_top1, W_top2, b_top2, W_top3)
    r_dense_features, ids, tbl_0, tbl_1, tbl_2, tbl_3, tbl_4, tbl_5, tbl_6, tbl_7, tbl_8, tbl_9, tbl_10, tbl_11, tbl_12, tbl_13, tbl_14, tbl_15, tbl_16, tbl_17, tbl_18, tbl_19, tbl_20, tbl_21, tbl_22, tbl_23, tbl_24, tbl_25, W_top1, b_top1, W_top2, b_top2, W_top3 = _rec_inputs()

    def _L0_rec_setup():
        import jax, jax.numpy as jnp
        import numpy as np
        NUM_SPARSE = 26
        EMBED_DIM = 128
        BATCH = 2048
        key = jax.random.key(seed)
        k1, k2 = jax.random.split(key)
        dense_features = jax.random.normal(k1, (BATCH, EMBED_DIM), dtype=jnp.float32)
        sparse_features = jax.random.normal(k2, (BATCH, NUM_SPARSE, EMBED_DIM), dtype=jnp.float32)
        return {'dense_features': dense_features, 'sparse_features': sparse_features}
    _L0_rec_all = _L0_rec_setup()
    _L0_rec_in = {k: v for k, v in _L0_rec_all.items() if k in ()}
    del _L0_rec_all
    return {'r_dense_features': r_dense_features, 'ids': ids, 'tbl_0': tbl_0, 'tbl_1': tbl_1, 'tbl_2': tbl_2, 'tbl_3': tbl_3, 'tbl_4': tbl_4, 'tbl_5': tbl_5, 'tbl_6': tbl_6, 'tbl_7': tbl_7, 'tbl_8': tbl_8, 'tbl_9': tbl_9, 'tbl_10': tbl_10, 'tbl_11': tbl_11, 'tbl_12': tbl_12, 'tbl_13': tbl_13, 'tbl_14': tbl_14, 'tbl_15': tbl_15, 'tbl_16': tbl_16, 'tbl_17': tbl_17, 'tbl_18': tbl_18, 'tbl_19': tbl_19, 'tbl_20': tbl_20, 'tbl_21': tbl_21, 'tbl_22': tbl_22, 'tbl_23': tbl_23, 'tbl_24': tbl_24, 'tbl_25': tbl_25, 'W_top1': W_top1, 'b_top1': b_top1, 'W_top2': W_top2, 'b_top2': b_top2, 'W_top3': W_top3}

def reference(r_dense_features, ids, tbl_0, tbl_1, tbl_2, tbl_3, tbl_4, tbl_5, tbl_6, tbl_7, tbl_8, tbl_9, tbl_10, tbl_11, tbl_12, tbl_13, tbl_14, tbl_15, tbl_16, tbl_17, tbl_18, tbl_19, tbl_20, tbl_21, tbl_22, tbl_23, tbl_24, tbl_25, W_top1, b_top1, W_top2, b_top2, W_top3):
    import jax
    import jax.numpy as jnp

    def _L0_rec_ref(dense_features, sparse_features):
        import jax, jax.numpy as jnp
        import numpy as np
        NUM_SPARSE = 26
        EMBED_DIM = 128
        BATCH = 2048
        F = NUM_SPARSE + 1
        combined = jnp.concatenate([dense_features[:, None, :], sparse_features], axis=1)
        interactions = jnp.einsum('bfd,bgd->bfg', combined, combined)
        iu, ju = jnp.triu_indices(F, k=1)
        interactions_flat = interactions[:, iu, ju]
        return jnp.concatenate([dense_features, interactions_flat], axis=1)
    e = jnp.stack([tbl_0[ids[:, 0]], tbl_1[ids[:, 1]], tbl_2[ids[:, 2]], tbl_3[ids[:, 3]], tbl_4[ids[:, 4]], tbl_5[ids[:, 5]], tbl_6[ids[:, 6]], tbl_7[ids[:, 7]], tbl_8[ids[:, 8]], tbl_9[ids[:, 9]], tbl_10[ids[:, 10]], tbl_11[ids[:, 11]], tbl_12[ids[:, 12]], tbl_13[ids[:, 13]], tbl_14[ids[:, 14]], tbl_15[ids[:, 15]], tbl_16[ids[:, 16]], tbl_17[ids[:, 17]], tbl_18[ids[:, 18]], tbl_19[ids[:, 19]], tbl_20[ids[:, 20]], tbl_21[ids[:, 21]], tbl_22[ids[:, 22]], tbl_23[ids[:, 23]], tbl_24[ids[:, 24]], tbl_25[ids[:, 25]]], axis=1)
    z = _L0_rec_ref(r_dense_features, e)
    z = z.reshape(z.shape[0], -1)
    h = jnp.concatenate([z, r_dense_features], axis=1)
    h = jnp.maximum(h @ W_top1 + b_top1, 0.0)
    h = jnp.maximum(h @ W_top2 + b_top2, 0.0)
    y = h @ W_top3
    return y

_drawn_inputs = setup_inputs


def setup_inputs(seed=0):
    import zlib

    import numpy as np

    out = dict(_drawn_inputs(seed))
    spreads = {'b_top1': (0.0, 0.1), 'b_top2': (0.0, 0.1)}
    factors = {}
    for name, (base, spread) in spreads.items():
        noise = np.random.default_rng([zlib.crc32(name.encode()), seed]).standard_normal(out[name].shape)
        drawn = base * np.exp(spread * noise) if base else spread * noise
        out[name] = jnp.asarray(drawn.astype(out[name].dtype))
    for name, factor in factors.items():
        out[name] = (out[name] * factor).astype(out[name].dtype)
    return out
```

```python
from contextlib import ExitStack

import concourse.bass as bass
from concourse import mybir

P = 128
TABLES = 26
FIELDS = TABLES + 1
SLOTS = 32
D = 128
BATCH = 512
TILES = BATCH // P
QUAD = P // SLOTS
COLS = FIELDS - 1
STRIP = 7
NB = P // QUAD
PER_BANK = 4
GROUP = 8
GROUPS = NB // GROUP
H1, H2 = 512, 256
FG = 4
FGROUPS = [list(range(i, min(i + FG, FIELDS))) for i in range(0, FIELDS, FG)]


def pair_row(a, f):
    return D + a * FIELDS - a * (a + 1) // 2 + (f - a - 1)


def schedule():
    steps = []
    for t in range(TILES):
        for n in range(len(FGROUPS)):
            steps.append(("rows", t, n))
            if t and n == 1:
                steps.append(("layer1", t - 1, 0))
            if t and n == 2:
                steps.append(("hidden", t - 1, 0))
            if t and n == 3:
                steps.append(("layer2", t - 1, 0))
        steps.append(("gram", t, 0))
    for kind in ("layer1", "hidden", "layer2"):
        steps.append((kind, TILES - 1, 0))
    out, turn = [], 0
    for kind, t, n in steps:
        out.append((kind, t, n, turn))
        turn += kind in ("rows", "hidden")
    return out


SCHEDULE = schedule()


def dlrm_kernel(nc, A, out):
    fp32 = mybir.dt.float32
    i32 = mybir.dt.int32
    ALU = mybir.AluOpType
    ACT = mybir.ActivationFunctionType

    ctx = ExitStack()
    with ctx:
        def sb(name, shape, dt=fp32):
            return ctx.enter_context(nc.sbuf_tensor(name, shape, dt))

        def ps(name, shape):
            return ctx.enter_context(nc.psum_tensor(name, shape, fp32))

        def sem(name):
            return ctx.enter_context(nc.semaphore(name))

        idx = sb("idx", [P, TILES * TABLES], i32)
        rows = sb("rows", [P, TILES, TABLES, D])
        dense = sb("dense", [P, TILES, D])
        ct = sb("ct", [P, TILES, P, SLOTS])
        pairs = sb("pairs", [P, 2, STRIP, P])
        w1 = sb("w1", [P, STRIP + 1, H1])
        w1_last = sb("w1_last", [P, H1])
        w2 = sb("w2", [P, H1 // P, H2])
        w3 = sb("w3", [P, H2])
        b2 = sb("b2", [P, H2])
        ident = sb("ident", [P, P])
        h1 = sb("h1", [P, H1])
        h1t = sb("h1t", [P, H1 // P, P])
        h2 = sb("h2", [P, H2])
        h2w = sb("h2w", [P, H2])
        y = sb("y", [P, TILES])

        turn_ps = [ps(f"turn_ps{i}", [P, 512]) for i in range(2)]
        gram_ps = [ps(f"gram_ps{i}", [P, GROUP // PER_BANK, 512]) for i in range(2)]
        h1_ps = ps("h1_ps", [P, H1])
        h2_ps = ps("h2_ps", [P, 512])

        idx_in = sem("idx_in")
        dense_in = sem("dense_in")
        rows_in = [[sem(f"rows_in{t}_{n}") for n in range(len(FGROUPS))] for t in range(TILES)]
        w1_in = sem("w1_in")
        w1_zero = sem("w1_zero")
        w1_sum = sem("w1_sum")
        w2_in = sem("w2_in")
        tail_in = sem("tail_in")
        ident_zero = sem("ident_zero")
        ident_set = sem("ident_set")
        pads_set = sem("pads_set")
        turned = sem("turned")
        turn_read = sem("turn_read")
        gram_done = sem("gram_done")
        gram_read_a = sem("gram_read_a")
        gram_read_v = sem("gram_read_v")
        l1_done = sem("l1_done")
        h1_read = sem("h1_read")
        l2_done = sem("l2_done")
        h2_read = sem("h2_read")
        h2_relu = sem("h2_relu")
        y_set = sem("y_set")
        y_out = sem("y_out")

        GROUP_READS = QUAD // 2 * QUAD

        def evacuate(copy, t, g, quads, done):
            src = gram_ps[g % 2]
            for j in quads:
                for r in range(QUAD):
                    n = min(STRIP, COLS - STRIP * r)
                    o = pairs[SLOTS * r:SLOTS * r + FIELDS, t % 2, 0:n, :].rearrange(
                        "f q (g k b j) -> f q g k b j", j=QUAD, g=GROUPS, k=GROUP // PER_BANK)[:, :, g, :, :, j]
                    c0 = j * COLS + r * STRIP
                    for k in range(GROUP // PER_BANK):
                        i = src[SLOTS * j:SLOTS * j + FIELDS, k, 0:PER_BANK * QUAD * COLS].rearrange(
                            "f (b c) -> f c b", b=PER_BANK)[:, c0:c0 + n, :]
                        copy(o[:, :, k, :], i).then_inc(done, 1)

        READS = GROUP_READS * (GROUP // PER_BANK)

        block = ctx.enter_context(nc.Block())

        @block.sync
        def _(sp):
            sp.dma_start(idx[:, :], A["ids"].rearrange("(p t) f -> p (t f)", t=TILES)).then_inc(idx_in, 16)
            sp.dma_start(dense[:, :, :], A["r_dense_features"].rearrange("(p t) d -> p t d", t=TILES))\
              .then_inc(dense_in, 16)
            sp.dma_start(w1[:, STRIP, :], A["W_top1"][0:D, :]).then_inc(w1_in, 16)
            sp.dma_start(w1_last[:, :], A["W_top1"][D + FIELDS * (FIELDS - 1) // 2:, :]).then_inc(w1_in, 16)
            sp.wait_ge(w1_zero, 1)
            for a in range(COLS):
                at = SLOTS * (a // STRIP)
                sp.dma_start(w1[at + a + 1:at + FIELDS, a % STRIP, :],
                             A["W_top1"][pair_row(a, a + 1):pair_row(a, FIELDS - 1) + 1, :]).then_inc(w1_in, 16)
            sp.dma_start(w1[SLOTS * 3:SLOTS * 3 + 1, STRIP - 1, :],
                         A["b_top1"].rearrange("(a n) -> a n", a=1)).then_inc(w1_in, 16)
            sp.dma_start(w2[:, :, :], A["W_top2"].rearrange("(c p) n -> p c n", p=P)).then_inc(w2_in, 16)
            sp.dma_start(b2[:, :], A["b_top2"].rearrange("(a n) -> a n", a=1).to_broadcast([P, H2]))\
              .then_inc(tail_in, 16)
            sp.dma_start(w3[:, :], A["W_top3"].rearrange("n a -> a n").to_broadcast([P, H2])).then_inc(tail_in, 16)
            sp.wait_ge(y_set, TILES)
            sp.dma_start(out.rearrange("(p t) a -> p (t a)", t=TILES), y[:, :]).then_inc(y_out, 16)
            sp.wait_ge(y_out, 16)

        @block.gpsimd
        def _(pool):
            nc.gpsimd.memset(ident[:, :], 0.0).then_inc(ident_zero, 1)
            pool.wait_ge(ident_zero, 1)
            nc.gpsimd.affine_select(out=ident[:, :], in_=ident[:, :], compare_op=ALU.not_equal, fill=1.0, base=0,
                                    pattern=[[-1, P]], channel_multiplier=1).then_inc(ident_set, 1)
            pool.wait_ge(idx_in, 16)
            for t in range(TILES):
                for n, fields in enumerate(FGROUPS):
                    for f in fields:
                        if f:
                            c = t * TABLES + f - 1
                            nc.gpsimd.indirect_dma_start(
                                out=rows[:, t, f - 1, :], out_offset=None, in_=A[f"tbl_{f - 1}"][:, :],
                                in_offset=bass.IndirectOffsetOnAxis(ap=idx[:, c:c + 1], axis=0))\
                              .then_inc(rows_in[t][n], 16)

        @block.tensor
        def _(pe):
            pe.wait_ge(ident_set, 1)
            pe.wait_ge(dense_in, 16)
            pe.wait_ge(pads_set, 4)
            for kind, t, n, turn in SCHEDULE:
                if kind == "rows":
                    fields = FGROUPS[n]
                    pe.wait_ge(rows_in[t][n], 16 * sum(f > 0 for f in fields))
                    if turn >= 2:
                        pe.wait_ge(turn_read, turn - 1)
                    for i, f in enumerate(fields):
                        src = rows[:, t, f - 1, :] if f else dense[:, t, :]
                        mm = nc.tensor.transpose(turn_ps[turn % 2][:, i * P:(i + 1) * P], src, ident[:, :])
                    mm.then_inc(turned, 1)
                elif kind == "gram":
                    last_turn = max(s[3] for s in SCHEDULE if s[:2] == ("rows", t))
                    pe.wait_ge(turn_read, last_turn + 1)
                    for g in range(GROUPS):
                        used = t * GROUPS + g
                        if used >= 2:
                            pe.wait_ge(gram_read_a, READS * (used - 1))
                            pe.wait_ge(gram_read_v, READS * (used - 1))
                        for b in range(GROUP):
                            s = QUAD * (g * GROUP + b)
                            c = (b % PER_BANK) * QUAD * COLS
                            mm = nc.tensor.matmul(
                                gram_ps[g % 2][:, b // PER_BANK, c:c + QUAD * COLS].rearrange(
                                    "m (j a) -> m j a", j=QUAD),
                                ct[:, t, s:s + QUAD, :].rearrange("d j f -> d (j f)"),
                                ct[:, t, s:s + QUAD, 0:COLS], start=True, stop=True)
                        mm.then_inc(gram_done, 1)
                elif kind == "layer1":
                    pe.wait_ge(gram_read_a, READS * GROUPS * (t + 1))
                    pe.wait_ge(gram_read_v, READS * GROUPS * (t + 1))
                    if t == 0:
                        pe.wait_ge(w1_in, 16 * (COLS + 3))
                        pe.wait_ge(w1_sum, 1)
                    else:
                        pe.wait_ge(h1_read, t)
                    nc.tensor.matmul(h1_ps[:, :], ct[:, t, :, 0], w1[:, STRIP, :], start=True, stop=False)
                    for q in range(STRIP):
                        mm = nc.tensor.matmul(h1_ps[:, :], pairs[:, t % 2, q, :], w1[:, q, :],
                                              start=False, stop=q == STRIP - 1)
                    mm.then_inc(l1_done, 1)
                elif kind == "hidden":
                    pe.wait_ge(h1_read, t + 1)
                    pe.wait_ge(turn_read, turn - 1)
                    for c in range(H1 // P):
                        mm = nc.tensor.transpose(turn_ps[turn % 2][:, c * P:(c + 1) * P],
                                                 h1[:, c * P:(c + 1) * P], ident[:, :])
                    mm.then_inc(turned, 1)
                else:
                    hidden_turn = next(s[3] for s in SCHEDULE if s[:2] == ("hidden", t))
                    pe.wait_ge(turn_read, hidden_turn + 1)
                    if t == 0:
                        pe.wait_ge(w2_in, 16)
                    else:
                        pe.wait_ge(h2_read, t)
                    for c in range(H1 // P):
                        mm = nc.tensor.matmul(h2_ps[:, 0:H2], h1t[:, c, :], w2[:, c, :],
                                              start=c == 0, stop=c == H1 // P - 1)
                    mm.then_inc(l2_done, 1)

        @block.scalar
        def _(act):
            for kind, t, n, turn in SCHEDULE:
                if kind == "rows":
                    k = len(FGROUPS[n])
                    act.wait_ge(turned, turn + 1)
                    nc.scalar.copy(ct[:, t, :, FG * n:FG * n + k].rearrange("d s f -> d f s"),
                                   turn_ps[turn % 2][:, 0:k * P].rearrange("d (f s) -> d f s", f=k))\
                      .then_inc(turn_read, 1)
                elif kind == "gram":
                    for g in range(GROUPS):
                        act.wait_ge(gram_done, t * GROUPS + g + 1)
                        if t >= 2 and g == 0:
                            act.wait_ge(l1_done, t - 1)
                        evacuate(nc.scalar.copy, t, g, (0, 1), gram_read_a)
                elif kind == "hidden":
                    act.wait_ge(turned, turn + 1)
                    if t:
                        act.wait_ge(l2_done, t)
                    nc.scalar.activation(h1t[:, :, :].rearrange("p c s -> p (c s)"), turn_ps[turn % 2][:, :],
                                         ACT.Relu).then_inc(turn_read, 1)

        @block.vector
        def _(dve):
            nc.vector.memset(w1[:, 0:STRIP, :], 0.0).then_inc(w1_zero, 1)
            nc.vector.memset(ct[:, :, :, FIELDS:], 0.0).then_inc(pads_set, 1)
            nc.vector.memset(pairs[:, :, :, :], 0.0).then_inc(pads_set, 1)
            dve.wait_ge(pads_set, 2)
            for b in range(2):
                nc.vector.memset(pairs[SLOTS * 3:P, b, STRIP - 1, :], 1.0).then_inc(pads_set, 1)
            dve.wait_ge(pads_set, 4)
            dve.wait_ge(w1_in, 16 * (COLS + 3))
            nc.vector.tensor_tensor(w1[:, STRIP, :], w1[:, STRIP, :], w1_last[:, :], ALU.add).then_inc(w1_sum, 1)
            for kind, t, n, turn in SCHEDULE:
                if kind == "gram":
                    for g in range(GROUPS):
                        dve.wait_ge(gram_done, t * GROUPS + g + 1)
                        if t >= 2 and g == 0:
                            dve.wait_ge(l1_done, t - 1)
                        evacuate(nc.vector.tensor_copy, t, g, (2, 3), gram_read_v)
                elif kind == "layer1":
                    dve.wait_ge(l1_done, t + 1)
                    if t:
                        dve.wait_ge(turned, next(s[3] for s in SCHEDULE if s[:2] == ("hidden", t - 1)) + 1)
                    nc.vector.tensor_copy(h1[:, :], h1_ps[:, :]).then_inc(h1_read, 1)
                elif kind == "layer2":
                    dve.wait_ge(l2_done, t + 1)
                    if t == 0:
                        dve.wait_ge(tail_in, 32)
                    else:
                        dve.wait_ge(y_set, t)
                    nc.vector.tensor_tensor(h2[:, :], h2_ps[:, 0:H2], b2[:, :], ALU.add).then_inc(h2_read, 1)
                    dve.wait_ge(h2_read, t + 1)
                    nc.vector.scalar_tensor_tensor(out=h2w[:, :], in0=h2[:, :], scalar=0.0, in1=w3[:, :],
                                                   op0=ALU.max, op1=ALU.mult, accum_out=y[:, t:t + 1])\
                      .then_inc(y_set, 1)


_INS = ["r_dense_features", "ids"] + [f"tbl_{i}" for i in range(TABLES)] + ["W_top1", "b_top1", "W_top2", "b_top2", "W_top3"]
_OUT = ((BATCH, 1), "float32")


def kernel(**inputs):
    import numpy as _np
    import concourse.bacc as _bacc
    from concourse import mybir as _mybir
    from concourse.bass_utils import run_bass_kernel_spmd as _run

    nc = _bacc.Bacc("TRN2", target_bir_lowering=False, num_devices=1)
    arrays, aps = {}, {}
    for name in _INS:
        a = _np.ascontiguousarray(inputs[name])
        arrays[f"in_{name}_dram"] = a
        aps[name] = nc.dram_tensor(f"in_{name}_dram", a.shape, _mybir.dt.from_np(a.dtype), kind="ExternalInput").ap()
    shape, dtype = _OUT
    out = nc.dram_tensor("out_0_dram", shape, _mybir.dt.from_np(_np.dtype(dtype)), kind="ExternalOutput").ap()
    dlrm_kernel(nc, aps, out)
    r = _run(nc, [arrays], core_ids=[0])
    return r.results[0]["out_0_dram"]
```

```python
from contextlib import ExitStack

import concourse.bass as bass
from concourse import mybir

P = 128
TABLES = 26
FIELDS = TABLES + 1
SLOTS = 32
D = 128
BATCH = 512
TILES = BATCH // P
QUAD = P // SLOTS
CHUNKS = -(-FIELDS // QUAD)
PRODUCTS = P // QUAD
BANK = 512
BUF = 2 * BANK
H1, H2 = 512, 256
W1_HALF = CHUNKS // 2

LOOKUP = [1, 3, 6, 13]
LOOKUP_ROWS = 1000
ROWS_EACH = LOOKUP_ROWS // P
REST = LOOKUP_ROWS - ROWS_EACH * P
ROW_CHUNKS = ROWS_EACH + 1
RAW = 3
LATE = FIELDS
GATHERED = [f for f in range(1, FIELDS) if f - 1 not in LOOKUP]

WHOLE = [(0, CHUNKS, 128)]
STAGES = WHOLE


def field_groups():
    groups = []
    for q0, q1, _ in STAGES:
        fields = [f for f in range(4 * q0, min(4 * q1, FIELDS)) if f == 0 or f in GATHERED]
        groups += [fields[i:i + 4] for i in range(0, len(fields), 4)]
    return groups


FGROUPS = field_groups()


def runs(fields):
    out, i = [], 0
    while i < len(fields):
        n = 1
        step = fields[i + 1] - fields[i] if i + 1 < len(fields) else 1
        while i + n < len(fields) and fields[i + n] - fields[i + n - 1] == step:
            n += 1
        out.append((i, fields[i], step, n))
        i += n
    return out


def pair_row(f, c):
    return D + f * FIELDS - f * (f + 1) // 2 + (c - f - 1)


def schedule():
    n = len(LOOKUP)
    steps = [("spread", 0, 0), ("upper", 0, 0), ("lower", 0, 0), ("spread", 1, 0), ("upper", 1, 0)]
    steps += [("spread", i, 0) for i in range(2, n)] + [("clear", 0, 0), ("clear", 1, 0)]
    first = [("rows", 0, g) for g in range(len(FGROUPS))]
    for i in range(n):
        steps.append(("lookup", i, 0))
        if i + 2 < n:
            steps.append(("upper", i + 2, 0))
        if i + 1 < n:
            steps.append(("lower", i + 1, 0))
        take = -(-len(first) // (n - i))
        steps += first[:take]
        first = first[take:]
    steps += [("gram", 0, 0), ("weights", 0, 0)]
    for t in range(1, TILES):
        groups = [("rows", t, g) for g in range(len(FGROUPS))]
        steps += groups[:1] + [("layer1", t - 1, 0)] + groups[1:3] + [("hidden", t - 1, 0)] + groups[3:4]
        steps += [("layer2", t - 1, 0)] + groups[4:] + [("gram", t, 0)]
    steps += [("layer1", TILES - 1, 0), ("hidden", TILES - 1, 0), ("layer2", TILES - 1, 0)]
    return steps


SCHEDULE = schedule()
TURN = {s: n for n, s in enumerate(s for s in SCHEDULE if s[0] in ("spread", "lookup", "rows", "hidden"))}


def stages(t):
    return STAGES if t == TILES - 1 else WHOLE


GROUPS = [(t, k, g) for t in range(TILES) for k in range(len(stages(t)))
          for g in range(PRODUCTS // (BUF // stages(t)[k][2]))]


def groups_through(t, k):
    return sum(g[:2] <= (t, k) for g in GROUPS)


def dlrm_kernel(nc, A, out):
    fp32 = mybir.dt.float32
    fp32r = mybir.dt.float32r
    fp16 = mybir.dt.float16
    i32 = mybir.dt.int32
    ALU = mybir.AluOpType
    ACT = mybir.ActivationFunctionType

    ctx = ExitStack()
    with ctx:
        def sb(name, shape, dt=fp32):
            return ctx.enter_context(nc.sbuf_tensor(name, shape, dt))

        def ps(name, shape):
            return ctx.enter_context(nc.psum_tensor(name, shape, fp32))

        def sem(name):
            return ctx.enter_context(nc.semaphore(name))

        idx = sb("idx", [P, TILES * TABLES], i32)
        idx_h = sb("idx_h", [P, TILES * TABLES], fp16)
        rows = sb("rows", [P, TILES, len(GATHERED), D])
        dense = sb("dense", [P, TILES, D])
        ct = sb("ct", [P, TILES, P, SLOTS])
        pairs = sb("pairs", [P, 2, CHUNKS, P])
        w1 = sb("w1", [P, CHUNKS + 1, H1])
        w1_last = sb("w1_last", [P, H1])
        w2 = sb("w2", [P, H1 // P, H2])
        w3 = sb("w3", [P, H2])
        b2 = sb("b2", [P, H2])
        ident = sb("ident", [P, P])
        ident_h = sb("ident_h", [P, P], fp16)
        row_no = sb("row_no", [P, ROW_CHUNKS])
        table = [sb(f"table{i}", [P, ROW_CHUNKS, D]) for i in range(RAW)]
        table_hi = [sb(f"table_hi{i}", [P, ROW_CHUNKS, D], fp32r) for i in range(2)]
        table_lo = [sb(f"table_lo{i}", [P, ROW_CHUNKS, D], fp32r) for i in range(2)]
        wanted = sb("wanted", [P, len(LOOKUP), BATCH], fp16)
        onehot = sb("onehot", [P, ROW_CHUNKS, BATCH], fp32r)
        h1 = sb("h1", [P, H1])
        h1t = sb("h1t", [P, H1 // P, P])
        h2 = sb("h2", [P, H2])
        h2w = sb("h2w", [P, H2])
        y = sb("y", [P, TILES])

        turn_ps = [ps(f"turn_ps{i}", [P, BANK]) for i in range(2)]
        gram_ps = [ps(f"gram_ps{i}", [P, BUF]) for i in range(2)]
        h1_ps = ps("h1_ps", [P, H1])
        h2_ps = ps("h2_ps", [P, BANK])

        idx_in = sem("idx_in")
        dense_in = sem("dense_in")
        table_in = [sem(f"table_in{i}") for i in range(RAW)]
        rows_in = [[sem(f"rows_in{t}_{n}") for n in range(len(FGROUPS))] for t in range(TILES)]
        w1_in = sem("w1_in")
        w1_zero = sem("w1_zero")
        w1_sum = sem("w1_sum")
        w2_in = sem("w2_in")
        tail_in = sem("tail_in")
        ident_zero = sem("ident_zero")
        ident_set = sem("ident_set")
        half_set = sem("half_set")
        table_zero = sem("table_zero")
        ct_zero = sem("ct_zero")
        pairs_zero = sem("pairs_zero")
        ones_set = sem("ones_set")
        turned = sem("turned")
        turn_read = sem("turn_read")
        hi_set = sem("hi_set")
        lo_set = sem("lo_set")
        onehot_set = sem("onehot_set")
        onehot_used = sem("onehot_used")
        gram_done = sem("gram_done")
        gram_read_a = sem("gram_read_a")
        gram_read_v = sem("gram_read_v")
        l1_done = sem("l1_done")
        h1_read = sem("h1_read")
        l2_done = sem("l2_done")
        h2_read = sem("h2_read")
        y_set = sem("y_set")
        y_out = sem("y_out")

        def evacuate(copy, group, quads, done):
            t, k, g = group
            q0, q1, step = stages(t)[k]
            n = BUF // step
            width = min(4 * q1, FIELDS) - 4 * q0
            src = gram_ps[GROUPS.index(group) % 2][:, :].rearrange("f (b c) -> f c b", c=step)
            for j in quads:
                for r in range(min(QUAD, width)):
                    nq = -(-(width - r) // QUAD)
                    o = pairs[SLOTS * r:SLOTS * r + FIELDS, t % 2, q0:q0 + nq, :].rearrange(
                        "f q (g b j) -> f q g b j", b=n, j=QUAD)[:, :, g, :, j]
                    i = src[SLOTS * j:SLOTS * j + FIELDS, j * width + r:(j + 1) * width:QUAD, :]
                    last = copy(o, i)
            last.then_inc(done, 1)

        block = ctx.enter_context(nc.Block())

        @block.sync
        def _(sp):
            def load_table(i):
                src = A[f"tbl_{LOOKUP[i]}"]
                if i >= RAW:
                    sp.wait_ge(hi_set, i - RAW + 1)
                    sp.wait_ge(lo_set, i - RAW + 1)
                sp.dma_start(table[i % RAW][:, 0:ROWS_EACH, :],
                             src[0:P * ROWS_EACH, :].rearrange("(p c) d -> p c d", c=ROWS_EACH))\
                  .then_inc(table_in[i % RAW], 16)
                sp.dma_start(table[i % RAW][0:REST, ROWS_EACH, :], src[P * ROWS_EACH:, :])\
                  .then_inc(table_in[i % RAW], 16)

            def load_pair_weights(f):
                row = A["W_top1"]
                if f < LATE - 1:
                    at = SLOTS * (f % QUAD)
                    sp.dma_start(w1[at + f + 1:at + LATE, f // QUAD, :],
                                 row[pair_row(f, f + 1):pair_row(f, LATE), :]).then_inc(w1_in, 16)
                if LATE < FIELDS:
                    c = max(LATE, f + 1)
                    at = SLOTS * (c % QUAD) + f
                    sp.dma_start(w1[at:at + SLOTS * (FIELDS - 1 - c) + 1:SLOTS, CHUNKS - 1, :],
                                 row[pair_row(f, c):pair_row(f, FIELDS), :]).then_inc(w1_in, 16)

            sp.dma_start(idx[:, :], A["ids"].rearrange("(p t) f -> p (t f)", t=TILES)).then_inc(idx_in, 16)
            sp.wait_ge(table_zero, 1)
            load_table(0)
            load_table(1)
            sp.dma_start(dense[:, :, :], A["r_dense_features"].rearrange("(p t) d -> p t d", t=TILES))\
              .then_inc(dense_in, 16)
            load_table(2)
            sp.dma_start(w1[:, CHUNKS, :], A["W_top1"][0:D, :]).then_inc(w1_in, 16)
            sp.dma_start(w1_last[:, :], A["W_top1"][D + FIELDS * (FIELDS - 1) // 2:, :]).then_inc(w1_in, 16)
            sp.wait_ge(w1_zero, 2)
            f = 0
            for i in range(3, len(LOOKUP)):
                load_table(i)
                for f in range(f, min(f + 6, FIELDS - 1)):
                    load_pair_weights(f)
                f += 1
            for f in range(f, FIELDS - 1):
                load_pair_weights(f)
            sp.dma_start(w1[SLOTS * 3:SLOTS * 3 + 1, CHUNKS - 1, :],
                         A["b_top1"].rearrange("(a n) -> a n", a=1)).then_inc(w1_in, 16)
            sp.dma_start(w2[:, :, :], A["W_top2"].rearrange("(c p) n -> p c n", p=P)).then_inc(w2_in, 16)
            sp.dma_start(b2[:, :], A["b_top2"].rearrange("(a n) -> a n", a=1).to_broadcast([P, H2]))\
              .then_inc(tail_in, 16)
            sp.dma_start(w3[:, :], A["W_top3"].rearrange("n a -> a n").to_broadcast([P, H2])).then_inc(tail_in, 16)
            sp.wait_ge(y_set, TILES)
            sp.dma_start(out.rearrange("(p t) a -> p (t a)", t=TILES), y[:, :]).then_inc(y_out, 16)
            sp.wait_ge(y_out, 16)

        W1_LOADS = LATE - 1 + (FIELDS - 1 if LATE < FIELDS else 0) + 3

        @block.gpsimd
        def _(pool):
            nc.gpsimd.memset(ident[:, :], 0.0).then_inc(ident_zero, 1)
            pool.wait_ge(ident_zero, 1)
            nc.gpsimd.affine_select(out=ident[:, :], in_=ident[:, :], compare_op=ALU.not_equal, fill=1.0, base=0,
                                    pattern=[[-1, P]], channel_multiplier=1).then_inc(ident_set, 1)
            nc.gpsimd.iota(row_no[:, 0:ROWS_EACH], [[1, ROWS_EACH]], base=0, channel_multiplier=ROWS_EACH,
                           allow_small_or_imprecise_dtypes=True).then_inc(ident_set, 1)
            nc.gpsimd.iota(row_no[:, ROWS_EACH:], [[1, 1]], base=P * ROWS_EACH, channel_multiplier=1,
                           allow_small_or_imprecise_dtypes=True).then_inc(ident_set, 1)
            pool.wait_ge(idx_in, 16)
            for t in range(TILES):
                for n, fields in enumerate(FGROUPS):
                    for f in fields:
                        if f:
                            c = t * TABLES + f - 1
                            nc.gpsimd.indirect_dma_start(
                                out=rows[:, t, GATHERED.index(f), :], out_offset=None, in_=A[f"tbl_{f - 1}"][:, :],
                                in_offset=bass.IndirectOffsetOnAxis(ap=idx[:, c:c + 1], axis=0))\
                              .then_inc(rows_in[t][n], 16)

        @block.tensor
        def _(pe):
            pe.wait_ge(half_set, 2)
            for step in SCHEDULE:
                kind, t, n = step
                if step in TURN:
                    turn = TURN[step]
                    if turn >= 2:
                        pe.wait_ge(turn_read, turn - 1)
                    bank = turn_ps[turn % 2]
                if kind == "spread":
                    for tile in range(TILES):
                        c = tile * TABLES + LOOKUP[t]
                        mm = nc.tensor.matmul(bank[:, tile * P:(tile + 1) * P],
                                              idx_h[:, c:c + 1].to_broadcast([P, P]), ident_h[:, :],
                                              start=True, stop=True)
                    mm.then_inc(turned, 1)
                elif kind == "lookup":
                    pe.wait_ge(hi_set, t + 1)
                    pe.wait_ge(lo_set, t + 1)
                    for c in range(ROW_CHUNKS):
                        pe.wait_ge(onehot_set, ROW_CHUNKS * t + c + 1)
                        nc.tensor.matmul(bank[:, :], table_hi[t % 2][:, c, :], onehot[:, c, :],
                                         start=c == 0, stop=False)
                        mm = nc.tensor.matmul(bank[:, :], table_lo[t % 2][:, c, :], onehot[:, c, :],
                                              start=False, stop=c == ROW_CHUNKS - 1)
                        if c < ROW_CHUNKS - 1:
                            mm.then_inc(onehot_used, 1)
                    mm.then_inc(turned, 1)
                elif kind == "rows":
                    fields = FGROUPS[n]
                    if 0 in fields:
                        pe.wait_ge(dense_in, 16)
                    pe.wait_ge(rows_in[t][n], 16 * sum(f > 0 for f in fields))
                    if step == ("rows", 0, 0):
                        pe.wait_ge(ident_set, 3)
                    for i, f in enumerate(fields):
                        src = rows[:, t, GATHERED.index(f), :] if f else dense[:, t, :]
                        mm = nc.tensor.transpose(bank[:, i * P:(i + 1) * P], src, ident[:, :])
                    mm.then_inc(turned, 1)
                elif kind == "gram":
                    q0, q1, pitch = stages(t)[n]
                    f1 = min(4 * q1, FIELDS)
                    if t == 0:
                        pe.wait_ge(ct_zero, 1)
                    ready = max(TURN["rows", t, g] for g, fields in enumerate(FGROUPS) if fields[0] < f1)
                    pe.wait_ge(turn_read, max(ready, TURN["lookup", len(LOOKUP) - 1, 0]) + 1)
                    per = BUF // pitch
                    width = f1 - 4 * q0
                    for g in range(PRODUCTS // per):
                        used = GROUPS.index((t, n, g))
                        if used >= 2:
                            pe.wait_ge(gram_read_a, used - 1)
                            pe.wait_ge(gram_read_v, used - 1)
                        for b in range(per):
                            s = QUAD * (g * per + b)
                            mm = nc.tensor.matmul(
                                gram_ps[used % 2][:, b * pitch:b * pitch + QUAD * width].rearrange(
                                    "m (j a) -> m j a", j=QUAD),
                                ct[:, t, s:s + QUAD, :].rearrange("d j f -> d (j f)"),
                                ct[:, t, s:s + QUAD, 4 * q0:f1], start=True, stop=True)
                        mm.then_inc(gram_done, 1)
                elif kind == "layer1":
                    q0, q1, _ = stages(t)[n]
                    if q0 == 0:
                        if t == 0:
                            pe.wait_ge(w1_in, 16 * W1_LOADS)
                            pe.wait_ge(w1_sum, 1)
                            pe.wait_ge(ones_set, 1)
                        else:
                            pe.wait_ge(h1_read, t)
                        nc.tensor.matmul(h1_ps[:, :], ct[:, t, :, 0], w1[:, CHUNKS, :], start=True, stop=False)
                    pe.wait_ge(gram_read_a, groups_through(t, n))
                    pe.wait_ge(gram_read_v, groups_through(t, n))
                    for q in range(q0, q1):
                        mm = nc.tensor.matmul(h1_ps[:, :], pairs[:, t % 2, q, :], w1[:, q, :],
                                              start=False, stop=q == CHUNKS - 1)
                    if q1 == CHUNKS:
                        mm.then_inc(l1_done, 1)
                elif kind == "hidden":
                    pe.wait_ge(h1_read, t + 1)
                    for c in range(H1 // P):
                        mm = nc.tensor.transpose(bank[:, c * P:(c + 1) * P], h1[:, c * P:(c + 1) * P], ident[:, :])
                    mm.then_inc(turned, 1)
                elif kind == "layer2":
                    pe.wait_ge(turn_read, TURN["hidden", t, 0] + 1)
                    if t == 0:
                        pe.wait_ge(w2_in, 16)
                    else:
                        pe.wait_ge(h2_read, t)
                    for c in range(H1 // P):
                        mm = nc.tensor.matmul(h2_ps[:, 0:H2], h1t[:, c, :], w2[:, c, :],
                                              start=c == 0, stop=c == H1 // P - 1)
                    mm.then_inc(l2_done, 1)

        @block.scalar
        def _(act):
            nc.scalar.memzero(w1[:, W1_HALF:CHUNKS, :]).then_inc(w1_zero, 1)
            for step in SCHEDULE:
                kind, t, n = step
                if step in TURN:
                    turn = TURN[step]
                    act.wait_ge(turned, turn + 1)
                    bank = turn_ps[turn % 2]
                if kind == "clear" and t == 0:
                    nc.scalar.memzero(ct[:, :, :, FIELDS:]).then_inc(ct_zero, 1)
                elif kind == "clear":
                    nc.scalar.memzero(pairs[:, :, :, :]).then_inc(pairs_zero, 1)
                elif kind == "spread":
                    nc.scalar.copy(wanted[:, t, :], bank[:, :]).then_inc(turn_read, 1)
                elif kind == "upper":
                    act.wait_ge(table_in[t % RAW], 32 * (t // RAW + 1))
                    if t >= 2:
                        act.wait_ge(turned, TURN["lookup", t - 2, 0] + 1)
                    nc.scalar.copy(table_hi[t % 2][:, :, :], table[t % RAW][:, :, :]).then_inc(hi_set, 1)
                elif kind == "lookup":
                    nc.scalar.copy(ct[:, :, :, LOOKUP[t] + 1],
                                   bank[:, :].rearrange("d (t s) -> d t s", t=TILES)).then_inc(turn_read, 1)
                elif kind == "rows":
                    for i, f, stride, k in runs(FGROUPS[n]):
                        last = nc.scalar.copy(ct[:, t, :, f:f + stride * (k - 1) + 1:stride].rearrange(
                            "d s f -> d f s"), bank[:, i * P:(i + k) * P].rearrange("d (f s) -> d f s", f=k))
                    last.then_inc(turn_read, 1)
                elif kind == "gram":
                    for group in GROUPS:
                        if group[:2] == (t, n):
                            act.wait_ge(gram_done, GROUPS.index(group) + 1)
                            if t >= 2:
                                act.wait_ge(l1_done, t - 1)
                            evacuate(nc.scalar.copy, group, (0, 1), gram_read_a)
                elif kind == "hidden":
                    if t:
                        act.wait_ge(l2_done, t)
                    nc.scalar.activation(h1t[:, :, :].rearrange("p c s -> p (c s)"), bank[:, :],
                                         ACT.Relu).then_inc(turn_read, 1)

        @block.vector
        def _(dve):
            for i in range(RAW):
                last = nc.vector.memset(table[i][96:P, ROWS_EACH, :], 0.0)
            last.then_inc(table_zero, 1)
            nc.vector.memset(w1[:, 0:W1_HALF, :], 0.0).then_inc(w1_zero, 1)
            dve.wait_ge(idx_in, 16)
            nc.vector.tensor_copy(idx_h[:, :], idx[:, :]).then_inc(half_set, 1)
            dve.wait_ge(ident_set, 3)
            nc.vector.tensor_copy(ident_h[:, :], ident[:, :]).then_inc(half_set, 1)
            for step in SCHEDULE:
                kind, t, n = step
                if kind == "lower":
                    dve.wait_ge(hi_set, t + 1)
                    if t >= 2:
                        dve.wait_ge(turned, TURN["lookup", t - 2, 0] + 1)
                    nc.vector.tensor_tensor(table_lo[t % 2][:, :, :], table[t % RAW][:, :, :],
                                            table_hi[t % 2][:, :, :].bitcast(fp32), ALU.subtract).then_inc(lo_set, 1)
                elif kind == "lookup":
                    dve.wait_ge(turn_read, TURN["spread", t, 0] + 1)
                    for c in range(ROW_CHUNKS):
                        if t:
                            if c < ROW_CHUNKS - 1:
                                dve.wait_ge(onehot_used, (ROW_CHUNKS - 1) * (t - 1) + c + 1)
                            else:
                                dve.wait_ge(turned, TURN["lookup", t - 1, 0] + 1)
                        nc.vector.tensor_scalar(onehot[:, c, :], wanted[:, t, :], row_no[:, c:c + 1], None,
                                                ALU.is_equal).then_inc(onehot_set, 1)
                elif kind == "gram":
                    if t == 0:
                        dve.wait_ge(pairs_zero, 1)
                        for b in range(2):
                            last = nc.vector.memset(pairs[SLOTS * 3:P, b, CHUNKS - 1, :], 1.0)
                        last.then_inc(ones_set, 1)
                    for group in GROUPS:
                        if group[:2] == (t, n):
                            dve.wait_ge(gram_done, GROUPS.index(group) + 1)
                            if t >= 2:
                                dve.wait_ge(l1_done, t - 1)
                            evacuate(nc.vector.tensor_copy, group, (2, 3), gram_read_v)
                elif kind == "weights":
                    dve.wait_ge(w1_in, 16 * W1_LOADS)
                    nc.vector.tensor_tensor(w1[:, CHUNKS, :], w1[:, CHUNKS, :], w1_last[:, :],
                                            ALU.add).then_inc(w1_sum, 1)
                elif kind == "layer1" and stages(t)[n][1] == CHUNKS:
                    dve.wait_ge(l1_done, t + 1)
                    if t:
                        dve.wait_ge(turned, TURN["hidden", t - 1, 0] + 1)
                    nc.vector.tensor_copy(h1[:, :], h1_ps[:, :]).then_inc(h1_read, 1)
                elif kind == "layer2":
                    dve.wait_ge(l2_done, t + 1)
                    if t == 0:
                        dve.wait_ge(tail_in, 32)
                    else:
                        dve.wait_ge(y_set, t)
                    nc.vector.tensor_tensor(h2[:, :], h2_ps[:, 0:H2], b2[:, :], ALU.add).then_inc(h2_read, 1)
                    dve.wait_ge(h2_read, t + 1)
                    nc.vector.scalar_tensor_tensor(out=h2w[:, :], in0=h2[:, :], scalar=0.0, in1=w3[:, :],
                                                   op0=ALU.max, op1=ALU.mult, accum_out=y[:, t:t + 1])\
                      .then_inc(y_set, 1)


_INS = ["r_dense_features", "ids"] + [f"tbl_{i}" for i in range(TABLES)] + ["W_top1", "b_top1", "W_top2", "b_top2", "W_top3"]
_OUT = ((BATCH, 1), "float32")


def kernel(**inputs):
    import numpy as _np
    import concourse.bacc as _bacc
    from concourse import mybir as _mybir
    from concourse.bass_utils import run_bass_kernel_spmd as _run

    nc = _bacc.Bacc("TRN2", target_bir_lowering=False, num_devices=1)
    arrays, aps = {}, {}
    for name in _INS:
        a = _np.ascontiguousarray(inputs[name])
        arrays[f"in_{name}_dram"] = a
        aps[name] = nc.dram_tensor(f"in_{name}_dram", a.shape, _mybir.dt.from_np(a.dtype), kind="ExternalInput").ap()
    shape, dtype = _OUT
    out = nc.dram_tensor("out_0_dram", shape, _mybir.dt.from_np(_np.dtype(dtype)), kind="ExternalOutput").ap()
    dlrm_kernel(nc, aps, out)
    r = _run(nc, [arrays], core_ids=[0])
    return r.results[0]["out_0_dram"]
```

```python
from contextlib import ExitStack

import concourse.bass as bass
from concourse import mybir

P = 128
TABLES = 26
FIELDS = TABLES + 1
SLOTS = 32
D = 128
BATCH = 512
TILES = BATCH // P
QUAD = P // SLOTS
CHUNKS = -(-FIELDS // QUAD)
PRODUCTS = P // QUAD
GRAM_ROWS = P - SLOTS + FIELDS
BANK = 512
BUF = 2 * BANK
H1, H2 = 512, 256
HALF = H1 // 2
ORDER = [CHUNKS] + list(range(CHUNKS))
GRAM_EACH = BUF // P
GRAM_GROUPS = PRODUCTS // GRAM_EACH
SAMPLES = P // GRAM_GROUPS
PIECES = 1 + GRAM_GROUPS
W1_EACH = 2
W1_PIECES = (CHUNKS + 1) // W1_EACH

LOOKUP = [1, 3, 6, 13, 18, 19, 20]
LOOKUP_ROWS = 1000
ROWS_EACH = LOOKUP_ROWS // P
REST = LOOKUP_ROWS - ROWS_EACH * P
ROW_CHUNKS = ROWS_EACH + 1
RAW = 2
BY_VECTOR = ROW_CHUNKS - 1
WANTED = 3
ONEHOTS = 6
WARM = 10
GATHERED = [f for f in range(1, FIELDS) if f - 1 not in LOOKUP]

TRANSPOSED = [0] + GATHERED
FGROUPS = [TRANSPOSED[i:i + BANK // P] for i in range(0, len(TRANSPOSED), BANK // P)]


def runs(fields):
    out, i = [], 0
    while i < len(fields):
        n = 1
        step = fields[i + 1] - fields[i] if i + 1 < len(fields) else 1
        while i + n < len(fields) and fields[i + n] - fields[i + n - 1] == step:
            n += 1
        out.append((i, fields[i], step, n))
        i += n
    return out


def pair_row(f, c):
    return D + f * FIELDS - f * (f + 1) // 2 + (c - f - 1)


def schedule():
    n = len(LOOKUP)
    steps = [("spread", 0, 0), ("upper", 0, 0), ("onehot", 0, 0), ("lower", 0, 0), ("spread", 1, 0), ("upper", 1, 0),
             ("onehot", 1, 0), ("clear", 0, 0)]
    first = [("rows", 0, g) for g in range(len(FGROUPS))]
    for i in range(n):
        steps.append(("lookup", i, 0))
        if i + 2 < n:
            steps += [("upper", i + 2, 0), ("spread", i + 2, 0), ("onehot", i + 2, 0)]
        if i + 1 < n:
            steps.append(("lower", i + 1, 0))
        take = -(-len(first) // (n - i))
        steps += first[:take]
        first = first[take:]
    steps += [("weights", 0, 0), ("rows", 1, 0), ("rows", 1, 1)] + [("gram", 0, g) for g in range(GRAM_GROUPS)]
    steps += [("weights", 0, i) for i in range(1, W1_PIECES + 1)]
    for t in range(1, TILES):
        layer1_after = len(FGROUPS) - 2 if t < TILES - 1 else len(FGROUPS) - 3
        for g in range(len(FGROUPS)):
            if ("rows", t, g) not in steps:
                steps.append(("rows", t, g))
            if g == layer1_after:
                steps.append(("layer1", t - 1, 0))
        if t < TILES - 1:
            steps.append(("rows", t + 1, 0))
        steps += [("hidden", t - 1, 0), ("dense", t, 0)] + [("gram", t, g) for g in range(GRAM_GROUPS)]
        steps.append(("layer2", t - 1, 0))
    steps.append(("finish", TILES - 1, 0))
    return steps


SCHEDULE = schedule()
TURN = {s: n for n, s in enumerate(s for s in SCHEDULE if s[0] in ("spread", "rows", "hidden", "layer2"))}
TURN_BANKS = 3


def by_vector(step):
    return step[0] == "rows" and step[1] > 0 and step[2] % 2 == 1


def dlrm_kernel(nc, A, out):
    fp32 = mybir.dt.float32
    fp32r = mybir.dt.float32r
    fp16 = mybir.dt.float16
    i32 = mybir.dt.int32
    ALU = mybir.AluOpType
    ACT = mybir.ActivationFunctionType

    ctx = ExitStack()
    with ctx:
        def sb(name, shape, dt=fp32):
            return ctx.enter_context(nc.sbuf_tensor(name, shape, dt))

        def ps(name, shape):
            return ctx.enter_context(nc.psum_tensor(name, shape, fp32))

        def sem(name):
            return ctx.enter_context(nc.semaphore(name))

        idx = sb("idx", [P, TILES * TABLES], i32)
        idx_h = sb("idx_h", [P, TILES * TABLES], fp16)
        rows = sb("rows", [P, 2, len(GATHERED), D])
        dense = sb("dense", [P, TILES, D])
        ct = sb("ct", [P, TILES, P, SLOTS])
        pairs = sb("pairs", [P, CHUNKS, P])
        in_hi = sb("in_hi", [P, CHUNKS + 1, P], fp32r)
        in_lo = sb("in_lo", [P, CHUNKS + 1, P], fp32r)
        w1 = sb("w1", [P, CHUNKS + 1, H1])
        w1_hi = sb("w1_hi", [P, CHUNKS + 1, H1], fp32r)
        w1_lo = sb("w1_lo", [P, CHUNKS + 1, H1], fp32r)
        w1_last = sb("w1_last", [P, H1])
        w2 = sb("w2", [P, H1 // P, H2])
        w3 = sb("w3", [P, H2])
        b2 = sb("b2", [P, H2])
        ones = sb("ones", [P, P])
        ident = sb("ident", [P, P])
        ident_h = sb("ident_h", [P, P], fp16)
        row_no = sb("row_no", [P, ROW_CHUNKS])
        table = [sb(f"table{i}", [P, ROW_CHUNKS, D]) for i in range(RAW)]
        table_hi = [sb(f"table_hi{i}", [P, ROW_CHUNKS, D], fp32r) for i in range(2)]
        table_lo = [sb(f"table_lo{i}", [P, ROW_CHUNKS, D], fp32r) for i in range(2)]
        onehot = sb("onehot", [P, ONEHOTS, BATCH], fp32r)
        onehot_last = sb("onehot_last", [P, 2, BATCH], fp32r)
        distance = sb("distance", [P, BATCH])
        wanted = sb("wanted", [P, WANTED, BATCH], fp16)
        h1 = sb("h1", [P, H1])
        h1t = sb("h1t", [P, H1 // P, P])
        h2 = sb("h2", [P, H2])
        h2w = sb("h2w", [P, H2])
        y = sb("y", [P, TILES])

        turn_ps = [ps(f"turn_ps{i}", [P, BANK]) for i in range(TURN_BANKS)]
        gram_ps = [ps(f"gram_ps{i}", [P, BUF]) for i in range(2)]
        h1_ps = ps("h1_ps", [P, H1])

        idx_in = sem("idx_in")
        dense_in = sem("dense_in")
        table_in = [sem(f"table_in{i}") for i in range(RAW)]
        rows_in = [[sem(f"rows_in{t}_{n}") for n in range(len(FGROUPS))] for t in range(TILES)]
        w1_in = sem("w1_in")
        w1_zero = sem("w1_zero")
        w1_sum = sem("w1_sum")
        w2_in = sem("w2_in")
        tail_in = sem("tail_in")
        ones_set = sem("ones_set")
        y_set = sem("y_set")
        ident_zero = sem("ident_zero")
        ident_set = sem("ident_set")
        half_set = sem("half_set")
        table_zero = sem("table_zero")
        ct_zero = sem("ct_zero")
        pairs_zero = sem("pairs_zero")
        bias_row_set = sem("bias_row_set")
        turned = sem("turned")
        turn_read = [sem(f"turn_read{i}") for i in range(TURN_BANKS)]
        hi_set = sem("hi_set")
        lo_set = sem("lo_set")
        onehot_set = sem("onehot_set")
        distance_set = sem("distance_set")
        onehot_last_set = sem("onehot_last_set")
        onehot_used = sem("onehot_used")
        looked_up = sem("looked_up")
        lookup_read = sem("lookup_read")
        gram_done = sem("gram_done")
        gram_read_a = sem("gram_read_a")
        gram_read_v = sem("gram_read_v")
        in_hi_set = sem("in_hi_set")
        in_lo_set = sem("in_lo_set")
        w1_hi_set = sem("w1_hi_set")
        w1_lo_set = sem("w1_lo_set")
        half_done = sem("half_done")
        half_copied = sem("half_copied")
        half_turned = sem("half_turned")
        half_relu = sem("half_relu")
        l2_done = sem("l2_done")
        l1_done = sem("l1_done")
        h1_read = sem("h1_read")
        y_out = sem("y_out")

        def evacuate(copy, t, g, quads, done):
            src = gram_ps[(GRAM_GROUPS * t + g) % 2][:, :].rearrange("f (b c) -> f c b", c=P)
            for j in quads:
                for r in range(QUAD):
                    chunks = -(-(FIELDS - r) // QUAD)
                    o = pairs[SLOTS * r:SLOTS * r + FIELDS, 0:chunks, :].rearrange(
                        "f q (g b j) -> f q g b j", b=GRAM_EACH, j=QUAD)[:, :, g, :, j]
                    i = src[SLOTS * j:SLOTS * j + FIELDS, j * FIELDS + r:(j + 1) * FIELDS:QUAD, :]
                    last = copy(o, i)
            last.then_inc(done, 1)

        def place_rows(copy, step):
            _, t, n = step
            bank = turn_ps[TURN[step] % TURN_BANKS]
            for i, f, stride, k in runs(FGROUPS[n]):
                last = copy(ct[:, t, :, f:f + stride * (k - 1) + 1:stride].rearrange("d s f -> d f s"),
                            bank[:, i * P:(i + k) * P].rearrange("d (f s) -> d f s", f=k))
            last.then_inc(turn_read[TURN[step] % TURN_BANKS], 1)

        def wait_turn_read(eng, step):
            eng.wait_ge(turn_read[TURN[step] % TURN_BANKS], TURN[step] // TURN_BANKS + 1)

        def last_turns():
            return [max((s for s in TURN if TURN[s] % TURN_BANKS == b), key=TURN.get) for b in range(TURN_BANKS)]

        half_ps = [h1_ps, gram_ps[0]]
        half_bank = turn_ps[0:2]
        l2_bank = turn_ps[2]

        block = ctx.enter_context(nc.Block())

        @block.sync
        def _(sp):
            def load_table(i):
                src = A[f"tbl_{LOOKUP[i]}"]
                if i >= RAW:
                    sp.wait_ge(hi_set, i - RAW + 1)
                    sp.wait_ge(lo_set, i - RAW + 1)
                sp.dma_start(table[i % RAW][:, 0:ROWS_EACH, :],
                             src[0:P * ROWS_EACH, :].rearrange("(p c) d -> p c d", c=ROWS_EACH))\
                  .then_inc(table_in[i % RAW], 16)
                sp.dma_start(table[i % RAW][0:REST, ROWS_EACH, :], src[P * ROWS_EACH:, :])\
                  .then_inc(table_in[i % RAW], 16)

            def load_pair_weights(f):
                at = SLOTS * (f % QUAD)
                sp.dma_start(w1[at + f + 1:at + FIELDS, f // QUAD, :],
                             A["W_top1"][pair_row(f, f + 1):pair_row(f, FIELDS), :]).then_inc(w1_in, 16)

            sp.dma_start(idx[:, :], A["ids"].rearrange("(p t) f -> p (t f)", t=TILES)).then_inc(idx_in, 16)
            sp.wait_ge(table_zero, 1)
            load_table(0)
            load_table(1)
            sp.dma_start(dense[:, :, :], A["r_dense_features"].rearrange("(p t) d -> p t d", t=TILES))\
              .then_inc(dense_in, 16)
            sp.dma_start(w1[:, CHUNKS, :], A["W_top1"][0:D, :]).then_inc(w1_in, 16)
            sp.dma_start(w1_last[:, :], A["W_top1"][D + FIELDS * (FIELDS - 1) // 2:, :]).then_inc(w1_in, 16)
            sp.wait_ge(w1_zero, 2)
            each = -(-(FIELDS - 1) // (len(LOOKUP) - RAW + 1))
            for i in range(RAW, len(LOOKUP) + 1):
                for f in range(each * (i - RAW), min(each * (i - RAW + 1), FIELDS - 1)):
                    load_pair_weights(f)
                if i < len(LOOKUP):
                    load_table(i)
            sp.dma_start(w1[SLOTS * 3:SLOTS * 3 + 1, CHUNKS - 1, :],
                         A["b_top1"].rearrange("(a n) -> a n", a=1)).then_inc(w1_in, 16)
            sp.dma_start(w2[:, :, :], A["W_top2"].rearrange("(c p) n -> p c n", p=P)).then_inc(w2_in, 16)
            sp.dma_start(b2[:, :], A["b_top2"].rearrange("(a n) -> a n", a=1).to_broadcast([P, H2]))\
              .then_inc(tail_in, 16)
            sp.dma_start(w3[:, :], A["W_top3"].rearrange("n a -> a n").to_broadcast([P, H2])).then_inc(tail_in, 16)
            sp.wait_ge(y_set, TILES)
            sp.dma_start(out.rearrange("(p t) a -> p (t a)", t=TILES), y[:, :]).then_inc(y_out, 16)
            sp.wait_ge(y_out, 16)

        W1_LOADS = FIELDS - 1 + 3

        @block.gpsimd
        def _(pool):
            nc.gpsimd.memset(ident[:, :], 0.0).then_inc(ident_zero, 1)
            pool.wait_ge(ident_zero, 1)
            nc.gpsimd.affine_select(out=ident[:, :], in_=ident[:, :], compare_op=ALU.not_equal, fill=1.0, base=0,
                                    pattern=[[-1, P]], channel_multiplier=1).then_inc(ident_set, 1)
            nc.gpsimd.iota(row_no[:, 0:ROWS_EACH], [[1, ROWS_EACH]], base=0, channel_multiplier=ROWS_EACH,
                           allow_small_or_imprecise_dtypes=True).then_inc(ident_set, 1)
            nc.gpsimd.iota(row_no[:, ROWS_EACH:], [[1, 1]], base=P * ROWS_EACH, channel_multiplier=1,
                           allow_small_or_imprecise_dtypes=True).then_inc(ident_set, 1)
            nc.gpsimd.memset(pairs[:, :, :], 0.0).then_inc(pairs_zero, 1)
            pool.wait_ge(idx_in, 16)
            for t in range(TILES):
                for n, fields in enumerate(FGROUPS):
                    if t >= 2:
                        pool.wait_ge(turned, TURN["rows", t - 2, n] + 1)
                    for f in fields:
                        if f:
                            c = t * TABLES + f - 1
                            nc.gpsimd.indirect_dma_start(
                                out=rows[:, t % 2, GATHERED.index(f), :], out_offset=None, in_=A[f"tbl_{f - 1}"][:, :],
                                in_offset=bass.IndirectOffsetOnAxis(ap=idx[:, c:c + 1], axis=0))\
                              .then_inc(rows_in[t][n], 16)

        @block.tensor
        def _(pe):
            pe.wait_ge(half_set, 2)
            for step in SCHEDULE:
                kind, t, n = step
                if step in TURN:
                    turn = TURN[step]
                    if turn >= TURN_BANKS:
                        pe.wait_ge(turn_read[turn % TURN_BANKS], turn // TURN_BANKS)
                    bank = turn_ps[turn % TURN_BANKS]
                if kind == "spread":
                    for tile in range(TILES):
                        c = tile * TABLES + LOOKUP[t]
                        mm = nc.tensor.matmul(bank[:, tile * P:(tile + 1) * P],
                                              idx_h[:, c:c + 1].to_broadcast([P, P]), ident_h[:, :],
                                              start=True, stop=True)
                    mm.then_inc(turned, 1)
                elif kind == "lookup":
                    if t == 0:
                        for _ in range(WARM):
                            nc.tensor.matmul(h1_ps[:, 0:P], ident_h[:, :], ident_h[:, :], start=True, stop=True)
                    if t >= 2:
                        pe.wait_ge(lookup_read, t - 1)
                    pe.wait_ge(hi_set, t + 1)
                    for c0, c1 in ((0, ROW_CHUNKS // 2), (ROW_CHUNKS // 2, ROW_CHUNKS)):
                        for part in (table_hi, table_lo):
                            if part is table_lo and c0 == 0:
                                pe.wait_ge(lo_set, t + 1)
                            for c in range(c0, c1):
                                here = BY_VECTOR * t + c
                                if c < BY_VECTOR:
                                    if part is table_hi:
                                        pe.wait_ge(onehot_set, here + 1)
                                    chosen = onehot[:, here % ONEHOTS, :]
                                else:
                                    pe.wait_ge(onehot_last_set, t + 1)
                                    chosen = onehot_last[:, t % 2, :]
                                mm = nc.tensor.matmul(gram_ps[t % 2][:, 0:BATCH], part[t % 2][:, c, :], chosen,
                                                      start=part is table_hi and c == 0,
                                                      stop=part is table_lo and c == ROW_CHUNKS - 1)
                                if part is table_lo and c < BY_VECTOR:
                                    mm.then_inc(onehot_used, 1)
                    mm.then_inc(looked_up, 1)
                elif kind == "rows":
                    fields = FGROUPS[n]
                    if 0 in fields:
                        pe.wait_ge(dense_in, 16)
                    pe.wait_ge(rows_in[t][n], 16 * sum(f > 0 for f in fields))
                    if step == ("rows", 0, 0):
                        pe.wait_ge(ident_set, 3)
                    for i, f in enumerate(fields):
                        src = rows[:, t % 2, GATHERED.index(f), :] if f else dense[:, t, :]
                        mm = nc.tensor.transpose(bank[:, i * P:(i + 1) * P], src, ident[:, :])
                    mm.then_inc(turned, 1)
                elif kind == "gram":
                    if n == 0:
                        for g in range(len(FGROUPS)):
                            wait_turn_read(pe, ("rows", t, g))
                    if t == 0 and n == 0:
                        pe.wait_ge(ct_zero, 1)
                        pe.wait_ge(lookup_read, len(LOOKUP))
                    used = GRAM_GROUPS * t + n
                    if used >= 2:
                        pe.wait_ge(gram_read_a, used - 1)
                        pe.wait_ge(gram_read_v, used - 1)
                    for b in range(GRAM_EACH):
                        s = SAMPLES * n + QUAD * b
                        mm = nc.tensor.matmul(
                            gram_ps[used % 2][0:GRAM_ROWS, b * P:b * P + QUAD * FIELDS].rearrange(
                                "m (j a) -> m j a", j=QUAD),
                            ct[:, t, s:s + QUAD, :].rearrange("d j f -> d (j f)")[:, 0:GRAM_ROWS],
                            ct[:, t, s:s + QUAD, 0:FIELDS], start=True, stop=True)
                    mm.then_inc(gram_done, 1)
                elif kind == "finish":

                    pe.wait_ge(h1_read, t)

                    def upper_products(half):
                        cols = slice(half * HALF, (half + 1) * HALF)
                        for q in ORDER:
                            pe.wait_ge(in_hi_set, PIECES * (t - 1) + 1 if q == CHUNKS else PIECES * t)
                            nc.tensor.matmul(half_ps[half][:, 0:HALF], in_hi[:, q, :], w1_hi[:, q, cols],
                                             start=q == CHUNKS, stop=False)
                            nc.tensor.matmul(half_ps[half][:, 0:HALF], in_hi[:, q, :], w1_lo[:, q, cols],
                                             start=False, stop=False)

                    def lower_products(half):
                        cols = slice(half * HALF, (half + 1) * HALF)
                        pe.wait_ge(in_lo_set, PIECES * t)
                        for q in ORDER:
                            mm = nc.tensor.matmul(half_ps[half][:, 0:HALF], in_lo[:, q, :], w1_hi[:, q, cols],
                                                  start=False, stop=q == ORDER[-1])
                        mm.then_inc(half_done, 1)

                    def transposes(half):
                        pe.wait_ge(half_copied, half + 1)
                        for c in range(HALF // P):
                            at = half * HALF + c * P
                            mm = nc.tensor.transpose(half_bank[half][:, c * P:(c + 1) * P], h1[:, at:at + P], ident[:, :])
                        mm.then_inc(half_turned, 1)

                    def second_layer(chunks):
                        for c in chunks:
                            pe.wait_ge(half_relu, c * P // HALF + 1)
                            mm = nc.tensor.matmul(l2_bank[:, 0:H2], h1t[:, c, :], w2[:, c, :],
                                                  start=False, stop=c == H1 // P - 1)
                        return mm

                    upper_products(0)
                    lower_products(0)
                    upper_products(1)
                    for step_before in last_turns():
                        wait_turn_read(pe, step_before)
                    transposes(0)
                    lower_products(1)
                    pe.wait_ge(tail_in, 32)
                    pe.wait_ge(ones_set, 1)
                    nc.tensor.matmul(l2_bank[:, 0:H2], ones[0:1, :], b2[0:1, :], start=True, stop=False)
                    transposes(1)
                    second_layer(range(H1 // P)).then_inc(l2_done, 1)
                elif kind == "layer1":
                    if t:
                        pe.wait_ge(h1_read, t)
                    if t == 0:
                        pe.wait_ge(w1_in, 16 * W1_LOADS)
                        pe.wait_ge(w1_sum, 1)
                        nc.tensor.matmul(h1_ps[:, :], ct[:, t, :, 0], w1[:, CHUNKS, :], start=True, stop=False)
                        pe.wait_ge(bias_row_set, 1)
                        pe.wait_ge(gram_read_a, GRAM_GROUPS)
                        pe.wait_ge(gram_read_v, GRAM_GROUPS)
                        for q in range(CHUNKS):
                            mm = nc.tensor.matmul(h1_ps[:, :], pairs[:, q, :], w1[:, q, :],
                                                  start=False, stop=q == CHUNKS - 1)
                        mm.then_inc(l1_done, 1)
                        continue
                    if t == 1:
                        pe.wait_ge(w1_hi_set, W1_PIECES)
                        pe.wait_ge(w1_lo_set, W1_PIECES)
                    for q in ORDER:
                        pe.wait_ge(in_hi_set, PIECES * (t - 1) + 1 if q == CHUNKS else PIECES * t)
                        nc.tensor.matmul(h1_ps[:, :], in_hi[:, q, :], w1_hi[:, q, :], start=q == CHUNKS, stop=False)
                        nc.tensor.matmul(h1_ps[:, :], in_hi[:, q, :], w1_lo[:, q, :], start=False, stop=False)
                    pe.wait_ge(in_lo_set, PIECES * t)
                    for q in ORDER:
                        mm = nc.tensor.matmul(h1_ps[:, :], in_lo[:, q, :], w1_hi[:, q, :],
                                              start=False, stop=q == ORDER[-1])
                    mm.then_inc(l1_done, 1)
                elif kind == "hidden":
                    pe.wait_ge(h1_read, t + 1)
                    for c in range(H1 // P):
                        mm = nc.tensor.transpose(bank[:, c * P:(c + 1) * P], h1[:, c * P:(c + 1) * P], ident[:, :])
                    mm.then_inc(turned, 1)
                elif kind == "layer2":
                    if t == 0:
                        pe.wait_ge(w2_in, 16)
                    wait_turn_read(pe, ("hidden", t, 0))
                    for c in range(H1 // P):
                        mm = nc.tensor.matmul(bank[:, 0:H2], h1t[:, c, :], w2[:, c, :],
                                              start=c == 0, stop=c == H1 // P - 1)
                    mm.then_inc(turned, 1)

        @block.scalar
        def _(act):
            nc.scalar.memzero(w1[:, CHUNKS // 2:CHUNKS, :]).then_inc(w1_zero, 1)
            for step in SCHEDULE:
                kind, t, n = step
                if step in TURN and not by_vector(step) and kind != "layer2":
                    turn = TURN[step]
                    act.wait_ge(turned, turn + 1)
                    bank = turn_ps[turn % TURN_BANKS]
                if kind == "clear":
                    nc.scalar.memzero(ct[:, :, :, FIELDS:]).then_inc(ct_zero, 1)
                elif kind == "spread":
                    if t >= WANTED:
                        act.wait_ge(looked_up, t - WANTED + 1)
                    nc.scalar.copy(wanted[:, t % WANTED, :], bank[:, :]).then_inc(turn_read[turn % TURN_BANKS], 1)
                elif kind == "upper":
                    act.wait_ge(table_in[t % RAW], 32 * (t // RAW + 1))
                    if t >= 2:
                        act.wait_ge(looked_up, t - 1)
                    nc.scalar.copy(table_hi[t % 2][:, :, :], table[t % RAW][:, :, :]).then_inc(hi_set, 1)
                elif kind == "onehot":
                    if t == 0:
                        act.wait_ge(ones_set, 1)
                        act.wait_ge(ident_set, 3)
                    else:
                        act.wait_ge(onehot_last_set, t)
                    if t >= 2:
                        act.wait_ge(looked_up, t - 1)
                    wait_turn_read(act, ("spread", t, 0))
                    nc.scalar.activation(distance[:, :], wanted[:, t % WANTED, :], ACT.Abs, scale=-1.0,
                                         bias=row_no[:, BY_VECTOR:]).then_inc(distance_set, 1)
                    act.wait_ge(distance_set, t + 1)
                    nc.scalar.activation(onehot_last[:, t % 2, :], distance[:, :], ACT.Relu, scale=-1.0,
                                         bias=ones[:, 0:1]).then_inc(onehot_last_set, 1)
                elif kind == "lookup":
                    act.wait_ge(looked_up, t + 1)
                    nc.scalar.copy(ct[:, :, :, LOOKUP[t] + 1],
                                   gram_ps[t % 2][:, 0:BATCH].rearrange("d (t s) -> d t s", t=TILES))\
                      .then_inc(lookup_read, 1)
                elif kind == "rows" and not by_vector(step):
                    place_rows(nc.scalar.copy, step)
                elif kind == "gram":
                    group = GRAM_GROUPS * t + n
                    act.wait_ge(gram_done, group + 1)
                    if t == 0 and n == 0:
                        act.wait_ge(pairs_zero, 1)
                    elif t == 1:
                        act.wait_ge(l1_done, 1)
                    elif t:
                        act.wait_ge(in_lo_set, PIECES * (t - 1))
                    evacuate(nc.scalar.copy, t, n, (0, 1), gram_read_a)
                    if t:
                        act.wait_ge(gram_read_a, group + 1)
                        act.wait_ge(gram_read_v, group + 1)
                        part = slice(n * SAMPLES, (n + 1) * SAMPLES)
                        nc.scalar.copy(in_hi[:, 0:CHUNKS, part], pairs[:, :, part]).then_inc(in_hi_set, 1)
                elif kind == "weights" and n:
                    if n == 1:
                        act.wait_ge(w1_in, 16 * W1_LOADS)
                        act.wait_ge(w1_sum, 1)
                    part = slice((n - 1) * W1_EACH, n * W1_EACH)
                    nc.scalar.copy(w1_hi[:, part, :], w1[:, part, :]).then_inc(w1_hi_set, 1)
                elif kind == "dense":
                    act.wait_ge(l1_done, t)
                    wait_turn_read(act, ("rows", t, 0))
                    nc.scalar.copy(in_hi[:, CHUNKS, :], ct[:, t, :, 0]).then_inc(in_hi_set, 1)
                elif kind == "finish":
                    act.wait_ge(turned, TURN["layer2", t - 1, 0] + 1)
                    for half in range(2):
                        act.wait_ge(half_turned, half + 1)
                        part = h1t[:, half * HALF // P:(half + 1) * HALF // P, :].rearrange("p c s -> p (c s)")
                        nc.scalar.activation(part, half_bank[half][:, 0:HALF], ACT.Relu).then_inc(half_relu, 1)
                elif kind == "hidden":
                    if t:
                        act.wait_ge(turned, TURN["layer2", t - 1, 0] + 1)
                    nc.scalar.activation(h1t[:, :, :].rearrange("p c s -> p (c s)"), bank[:, :],
                                         ACT.Relu).then_inc(turn_read[turn % TURN_BANKS], 1)

        @block.vector
        def _(dve):
            def set_lower(i):
                dve.wait_ge(hi_set, i + 1)
                if i >= 2:
                    dve.wait_ge(looked_up, i - 1)
                nc.vector.tensor_tensor(table_lo[i % 2][:, :, :], table[i % RAW][:, :, :],
                                        table_hi[i % 2][:, :, :].bitcast(fp32), ALU.subtract).then_inc(lo_set, 1)

            def pairs_lower(t, g):
                dve.wait_ge(in_hi_set, PIECES * (t - 1) + 2 + g)
                part = slice(g * SAMPLES, (g + 1) * SAMPLES)
                nc.vector.tensor_tensor(in_lo[:, 0:CHUNKS, part], pairs[:, :, part],
                                        in_hi[:, 0:CHUNKS, part].bitcast(fp32), ALU.subtract).then_inc(in_lo_set, 1)

            for i in range(RAW):
                last = nc.vector.memset(table[i][96:P, ROWS_EACH, :], 0.0)
            last.then_inc(table_zero, 1)
            nc.vector.memset(w1[:, 0:CHUNKS // 2, :], 0.0).then_inc(w1_zero, 1)
            nc.vector.memset(ones[:, :], 1.0).then_inc(ones_set, 1)
            dve.wait_ge(idx_in, 16)
            nc.vector.tensor_copy(idx_h[:, :], idx[:, :]).then_inc(half_set, 1)
            dve.wait_ge(ident_set, 3)
            nc.vector.tensor_copy(ident_h[:, :], ident[:, :]).then_inc(half_set, 1)
            for step in SCHEDULE:
                kind, t, n = step
                if kind == "rows" and by_vector(step):
                    dve.wait_ge(turned, TURN[step] + 1)
                    place_rows(nc.vector.tensor_copy, step)
                elif kind == "lower" and t:
                    set_lower(t)
                elif kind == "lookup":
                    wait_turn_read(dve, ("spread", t, 0))
                    for c in range(BY_VECTOR):
                        if t == 0 and c == ROW_CHUNKS // 2:
                            set_lower(0)
                        here = BY_VECTOR * t + c
                        if here >= ONEHOTS:
                            dve.wait_ge(onehot_used, here - ONEHOTS + 1)
                        nc.vector.tensor_scalar(onehot[:, here % ONEHOTS, :], wanted[:, t % WANTED, :], row_no[:, c:c + 1],
                                                None, ALU.is_equal).then_inc(onehot_set, 1)
                elif kind == "gram":
                    if t == 0 and n == 0:
                        dve.wait_ge(pairs_zero, 1)
                        nc.vector.memset(pairs[SLOTS * 3:P, CHUNKS - 1, :], 1.0).then_inc(bias_row_set, 1)
                    dve.wait_ge(gram_done, GRAM_GROUPS * t + n + 1)
                    if t == 1:
                        dve.wait_ge(l1_done, 1)
                    evacuate(nc.vector.tensor_copy, t, n, (2, 3), gram_read_v)
                    if t and n:
                        pairs_lower(t, n - 1)
                    if t and n == GRAM_GROUPS - 1:
                        pairs_lower(t, n)
                elif kind == "weights" and n:
                    part = slice((n - 1) * W1_EACH, n * W1_EACH)
                    dve.wait_ge(w1_hi_set, n)
                    nc.vector.tensor_tensor(w1_lo[:, part, :], w1[:, part, :], w1_hi[:, part, :].bitcast(fp32),
                                            ALU.subtract).then_inc(w1_lo_set, 1)
                elif kind == "weights":
                    dve.wait_ge(w1_in, 16 * W1_LOADS)
                    nc.vector.tensor_tensor(w1[:, CHUNKS, :], w1[:, CHUNKS, :], w1_last[:, :],
                                            ALU.add).then_inc(w1_sum, 1)
                elif kind == "dense":
                    dve.wait_ge(in_hi_set, PIECES * (t - 1) + 1)
                    nc.vector.tensor_tensor(in_lo[:, CHUNKS, :], ct[:, t, :, 0], in_hi[:, CHUNKS, :].bitcast(fp32),
                                            ALU.subtract).then_inc(in_lo_set, 1)
                elif kind == "layer1":
                    dve.wait_ge(l1_done, t + 1)
                    if t:
                        dve.wait_ge(turned, TURN["hidden", t - 1, 0] + 1)
                    nc.vector.tensor_copy(h1[:, :], h1_ps[:, :]).then_inc(h1_read, 1)
                elif kind == "finish":
                    dve.wait_ge(turned, TURN["hidden", t - 1, 0] + 1)
                    for half in range(2):
                        dve.wait_ge(half_done, half + 1)
                        nc.vector.tensor_copy(h1[:, half * HALF:(half + 1) * HALF],
                                              half_ps[half][:, 0:HALF]).then_inc(half_copied, 1)
                    dve.wait_ge(l2_done, 1)
                    dve.wait_ge(y_set, t)
                    nc.vector.scalar_tensor_tensor(out=h2w[:, :], in0=l2_bank[:, 0:H2], scalar=0.0, in1=w3[:, :],
                                                   op0=ALU.max, op1=ALU.mult, accum_out=y[:, t:t + 1])\
                      .then_inc(y_set, 1)
                elif kind == "layer2":
                    dve.wait_ge(turned, TURN[step] + 1)
                    bank = TURN[step] % TURN_BANKS
                    if t == 0:
                        dve.wait_ge(tail_in, 32)
                    else:
                        dve.wait_ge(y_set, t)
                    nc.vector.tensor_tensor(h2[:, :], turn_ps[bank][:, 0:H2], b2[:, :], ALU.add)\
                      .then_inc(turn_read[bank], 1)
                    wait_turn_read(dve, step)
                    nc.vector.scalar_tensor_tensor(out=h2w[:, :], in0=h2[:, :], scalar=0.0, in1=w3[:, :],
                                                   op0=ALU.max, op1=ALU.mult, accum_out=y[:, t:t + 1])\
                      .then_inc(y_set, 1)


_INS = ["r_dense_features", "ids"] + [f"tbl_{i}" for i in range(TABLES)] + ["W_top1", "b_top1", "W_top2", "b_top2", "W_top3"]
_OUT = ((BATCH, 1), "float32")


def kernel(**inputs):
    import numpy as _np
    import concourse.bacc as _bacc
    from concourse import mybir as _mybir
    from concourse.bass_utils import run_bass_kernel_spmd as _run

    nc = _bacc.Bacc("TRN2", target_bir_lowering=False, num_devices=1)
    arrays, aps = {}, {}
    for name in _INS:
        a = _np.ascontiguousarray(inputs[name])
        arrays[f"in_{name}_dram"] = a
        aps[name] = nc.dram_tensor(f"in_{name}_dram", a.shape, _mybir.dt.from_np(a.dtype), kind="ExternalInput").ap()
    shape, dtype = _OUT
    out = nc.dram_tensor("out_0_dram", shape, _mybir.dt.from_np(_np.dtype(dtype)), kind="ExternalOutput").ap()
    dlrm_kernel(nc, aps, out)
    r = _run(nc, [arrays], core_ids=[0])
    return r.results[0]["out_0_dram"]
```
